# Optimizing a Trainium2 kernel written in Bass

```python
import numpy as np
import jax
import jax.numpy as jnp

def _softmax(x, axis=-1):
    return jax.nn.softmax(x, axis=axis)

def _gelu(x):
    return jax.nn.gelu(x, approximate=True)

def _silu(x):
    return jax.nn.silu(x)

def _sigmoid(x):
    return jax.nn.sigmoid(x)

def _layernorm(x, axis=-1, eps=1e-05):
    m = jnp.mean(x, axis=axis, keepdims=True)
    v = jnp.var(x, axis=axis, keepdims=True)
    return (x - m) / jnp.sqrt(v + eps)

def _scatter_add(tgt, idx, src, axis=0):
    return tgt.at[idx].add(src)

def _segment_sum(src, seg, n):
    return jax.ops.segment_sum(src, seg, n)
kernel_name = 'mk_dlrm_tower_d1_rec_r8_a443b3'

def setup_inputs(seed: int=0):
    np.random.seed(seed)
    _w = jnp.asarray

    def _rec_inputs():
        import jax
        import jax.numpy as jnp
        _tk = jax.random.key(seed)
        dense_ctx = jax.random.normal(jax.random.fold_in(_tk, 190), (512, 16), jnp.float32)
        ids = jnp.stack([jax.random.randint(jax.random.fold_in(_tk, 200 + f), (512,), 0, v, jnp.int32) for f, v in enumerate([1250, 1250, 1250, 1250, 1250, 1250, 12500, 1000, 1250, 1250, 1250, 1000, 12500, 1000, 1000, 1250, 12500, 1000, 12500, 12500, 1250, 1250, 1250, 1000, 1000, 1000, 1250, 1000, 1000, 1000, 12500, 1250])], axis=1)
        tbl_0 = 0.05 * jax.random.normal(jax.random.fold_in(_tk, 500 + 0), (1250, 256), jnp.float32)
        tbl_1 = 0.05 * jax.random.normal(jax.random.fold_in(_tk, 500 + 1), (1250, 256), jnp.float32)
        tbl_2 = 0.05 * jax.random.normal(jax.random.fold_in(_tk, 500 + 2), (1250, 256), jnp.float32)
        tbl_3 = 0.05 * jax.random.normal(jax.random.fold_in(_tk, 500 + 3), (1250, 256), jnp.float32)
        tbl_4 = 0.05 * jax.random.normal(jax.random.fold_in(_tk, 500 + 4), (1250, 256), jnp.float32)
        tbl_5 = 0.05 * jax.random.normal(jax.random.fold_in(_tk, 500 + 5), (1250, 256), jnp.float32)
        tbl_6 = 0.05 * jax.random.normal(jax.random.fold_in(_tk, 500 + 6), (12500, 256), jnp.float32)
        tbl_7 = 0.05 * jax.random.normal(jax.random.fold_in(_tk, 500 + 7), (1000, 256), jnp.float32)
        tbl_8 = 0.05 * jax.random.normal(jax.random.fold_in(_tk, 500 + 8), (1250, 256), jnp.float32)
        tbl_9 = 0.05 * jax.random.normal(jax.random.fold_in(_tk, 500 + 9), (1250, 256), jnp.float32)
        tbl_10 = 0.05 * jax.random.normal(jax.random.fold_in(_tk, 500 + 10), (1250, 256), jnp.float32)
        tbl_11 = 0.05 * jax.random.normal(jax.random.fold_in(_tk, 500 + 11), (1000, 256), jnp.float32)
        tbl_12 = 0.05 * jax.random.normal(jax.random.fold_in(_tk, 500 + 12), (12500, 256), jnp.float32)
        tbl_13 = 0.05 * jax.random.normal(jax.random.fold_in(_tk, 500 + 13), (1000, 256), jnp.float32)
        tbl_14 = 0.05 * jax.random.normal(jax.random.fold_in(_tk, 500 + 14), (1000, 256), jnp.float32)
        tbl_15 = 0.05 * jax.random.normal(jax.random.fold_in(_tk, 500 + 15), (1250, 256), jnp.float32)
        tbl_16 = 0.05 * jax.random.normal(jax.random.fold_in(_tk, 500 + 16), (12500, 256), jnp.float32)
        tbl_17 = 0.05 * jax.random.normal(jax.random.fold_in(_tk, 500 + 17), (1000, 256), jnp.float32)
        tbl_18 = 0.05 * jax.random.normal(jax.random.fold_in(_tk, 500 + 18), (12500, 256), jnp.float32)
        tbl_19 = 0.05 * jax.random.normal(jax.random.fold_in(_tk, 500 + 19), (12500, 256), jnp.float32)
        tbl_20 = 0.05 * jax.random.normal(jax.random.fold_in(_tk, 500 + 20), (1250, 256), jnp.float32)
        tbl_21 = 0.05 * jax.random.normal(jax.random.fold_in(_tk, 500 + 21), (1250, 256), jnp.float32)
        tbl_22 = 0.05 * jax.random.normal(jax.random.fold_in(_tk, 500 + 22), (1250, 256), jnp.float32)
        tbl_23 = 0.05 * jax.random.normal(jax.random.fold_in(_tk, 500 + 23), (1000, 256), jnp.float32)
        tbl_24 = 0.05 * jax.random.normal(jax.random.fold_in(_tk, 500 + 24), (1000, 256), jnp.float32)
        tbl_25 = 0.05 * jax.random.normal(jax.random.fold_in(_tk, 500 + 25), (1000, 256), jnp.float32)
        tbl_26 = 0.05 * jax.random.normal(jax.random.fold_in(_tk, 500 + 26), (1250, 256), jnp.float32)
        tbl_27 = 0.05 * jax.random.normal(jax.random.fold_in(_tk, 500 + 27), (1000, 256), jnp.float32)
        tbl_28 = 0.05 * jax.random.normal(jax.random.fold_in(_tk, 500 + 28), (1000, 256), jnp.float32)
        tbl_29 = 0.05 * jax.random.normal(jax.random.fold_in(_tk, 500 + 29), (1000, 256), jnp.float32)
        tbl_30 = 0.05 * jax.random.normal(jax.random.fold_in(_tk, 500 + 30), (12500, 256), jnp.float32)
        tbl_31 = 0.05 * jax.random.normal(jax.random.fold_in(_tk, 500 + 31), (1250, 256), jnp.float32)
        _rk = jax.random.fold_in(_tk, 7)
        W_top1 = 0.0441942 * jax.random.normal(jax.random.fold_in(_tk, 801), (512, 512), jnp.float32)
        W_top2 = 0.0441942 * jax.random.normal(jax.random.fold_in(_tk, 802), (512, 256), jnp.float32)
        W_top3 = 0.0625 * jax.random.normal(jax.random.fold_in(_tk, 803), (256, 1), jnp.float32)
        b_top1 = jnp.zeros((512,), jnp.float32)
        b_top2 = jnp.zeros((256,), jnp.float32)
        return (dense_ctx, ids, tbl_0, tbl_1, tbl_2, tbl_3, tbl_4, tbl_5, tbl_6, tbl_7, tbl_8, tbl_9, tbl_10, tbl_11, tbl_12, tbl_13, tbl_14, tbl_15, tbl_16, tbl_17, tbl_18, tbl_19, tbl_20, tbl_21, tbl_22, tbl_23, tbl_24, tbl_25, tbl_26, tbl_27, tbl_28, tbl_29, tbl_30, tbl_31, W_top1, b_top1, W_top2, b_top2, W_top3)
    dense_ctx, ids, tbl_0, tbl_1, tbl_2, tbl_3, tbl_4, tbl_5, tbl_6, tbl_7, tbl_8, tbl_9, tbl_10, tbl_11, tbl_12, tbl_13, tbl_14, tbl_15, tbl_16, tbl_17, tbl_18, tbl_19, tbl_20, tbl_21, tbl_22, tbl_23, tbl_24, tbl_25, tbl_26, tbl_27, tbl_28, tbl_29, tbl_30, tbl_31, W_top1, b_top1, W_top2, b_top2, W_top3 = _rec_inputs()

    def _L0_rec_setup():
        import jax, jax.numpy as jnp
        import numpy as np
        B, N, D = (1024, 32, 256)
        key = jax.random.key(seed)
        x = jax.random.normal(key, (B, N, D), dtype=jnp.float32)
        return {'x': x}
    _L0_rec_all = _L0_rec_setup()
    _L0_rec_in = {k: v for k, v in _L0_rec_all.items() if k in ()}
    del _L0_rec_all
    return {'dense_ctx': dense_ctx, 'ids': ids, 'tbl_0': tbl_0, 'tbl_1': tbl_1, 'tbl_2': tbl_2, 'tbl_3': tbl_3, 'tbl_4': tbl_4, 'tbl_5': tbl_5, 'tbl_6': tbl_6, 'tbl_7': tbl_7, 'tbl_8': tbl_8, 'tbl_9': tbl_9, 'tbl_10': tbl_10, 'tbl_11': tbl_11, 'tbl_12': tbl_12, 'tbl_13': tbl_13, 'tbl_14': tbl_14, 'tbl_15': tbl_15, 'tbl_16': tbl_16, 'tbl_17': tbl_17, 'tbl_18': tbl_18, 'tbl_19': tbl_19, 'tbl_20': tbl_20, 'tbl_21': tbl_21, 'tbl_22': tbl_22, 'tbl_23': tbl_23, 'tbl_24': tbl_24, 'tbl_25': tbl_25, 'tbl_26': tbl_26, 'tbl_27': tbl_27, 'tbl_28': tbl_28, 'tbl_29': tbl_29, 'tbl_30': tbl_30, 'tbl_31': tbl_31, 'W_top1': W_top1, 'b_top1': b_top1, 'W_top2': W_top2, 'b_top2': b_top2, 'W_top3': W_top3}

def reference(dense_ctx, ids, tbl_0, tbl_1, tbl_2, tbl_3, tbl_4, tbl_5, tbl_6, tbl_7, tbl_8, tbl_9, tbl_10, tbl_11, tbl_12, tbl_13, tbl_14, tbl_15, tbl_16, tbl_17, tbl_18, tbl_19, tbl_20, tbl_21, tbl_22, tbl_23, tbl_24, tbl_25, tbl_26, tbl_27, tbl_28, tbl_29, tbl_30, tbl_31, W_top1, b_top1, W_top2, b_top2, W_top3):
    import jax
    import jax.numpy as jnp

    def _L0_rec_ref(x):
        import jax, jax.numpy as jnp
        import numpy as np
        B, N, D = (1024, 32, 256)
        'Second-order feature interaction (DLRM dot interaction).\n\n            Computes dot(x_i, x_j) for all field pairs i < j (self_interaction=False),\n            flattened in row-major upper-triangular order -> [B, N*(N-1)/2].\n            Matches tf.boolean_mask(dot_products, strictly_upper_mask) ordering.\n            '
        b, n, d = x.shape
        iu, ju = jnp.triu_indices(n, k=1)
        dots = jnp.einsum('bnd,bmd->bnm', x, x)
        return dots[:, iu, ju]
    e = jnp.stack([tbl_0[ids[:, 0]], tbl_1[ids[:, 1]], tbl_2[ids[:, 2]], tbl_3[ids[:, 3]], tbl_4[ids[:, 4]], tbl_5[ids[:, 5]], tbl_6[ids[:, 6]], tbl_7[ids[:, 7]], tbl_8[ids[:, 8]], tbl_9[ids[:, 9]], tbl_10[ids[:, 10]], tbl_11[ids[:, 11]], tbl_12[ids[:, 12]], tbl_13[ids[:, 13]], tbl_14[ids[:, 14]], tbl_15[ids[:, 15]], tbl_16[ids[:, 16]], tbl_17[ids[:, 17]], tbl_18[ids[:, 18]], tbl_19[ids[:, 19]], tbl_20[ids[:, 20]], tbl_21[ids[:, 21]], tbl_22[ids[:, 22]], tbl_23[ids[:, 23]], tbl_24[ids[:, 24]], tbl_25[ids[:, 25]], tbl_26[ids[:, 26]], tbl_27[ids[:, 27]], tbl_28[ids[:, 28]], tbl_29[ids[:, 29]], tbl_30[ids[:, 30]], tbl_31[ids[:, 31]]], axis=1)
    z = _L0_rec_ref(e)
    z = z.reshape(z.shape[0], -1)
    h = jnp.concatenate([z, dense_ctx], axis=1)
    h = jnp.maximum(h @ W_top1 + b_top1, 0.0)
    h = jnp.maximum(h @ W_top2 + b_top2, 0.0)
    y = h @ W_top3
    return y

_drawn_inputs = setup_inputs


def setup_inputs(seed=0):
    import zlib

    import numpy as np

    out = dict(_drawn_inputs(seed))
    spreads = {'b_top1': (0.0, 0.1), 'b_top2': (0.0, 0.1)}
    factors = {}
    for name, (base, spread) in spreads.items():
        noise = np.random.default_rng([zlib.crc32(name.encode()), seed]).standard_normal(out[name].shape)
        drawn = base * np.exp(spread * noise) if base else spread * noise
        out[name] = jnp.asarray(drawn.astype(out[name].dtype))
    for name, factor in factors.items():
        out[name] = (out[name] * factor).astype(out[name].dtype)
    return out
```

```python
from contextlib import ExitStack

import concourse.bass as bass
from concourse import mybir

F32 = mybir.dt.float32
I32 = mybir.dt.int32
ALU = mybir.AluOpType
ACT = mybir.ActivationFunctionType

P = 128
BATCH = 512
FIELDS = 32
DIM = 256
DENSE = 16
HID1 = 512
HID2 = 256
KC = DIM // P
SPG = P // FIELDS
GPC = 16
CHUNK = GPC * SPG
CHUNKS = BATCH // CHUNK
PAIRS = GPC // 2
HALF = GPC // 2
PPH = HALF // 2
JQ = P // FIELDS
JJ = FIELDS // JQ

N1 = HID1 // P
N2 = HID2 // P


def dlrm_tower(nc, ids, row_base, tables, dense, w1, b1, w2, b2, w3, out):
    ctx = ExitStack()
    with ctx:
        def sb(name, shape, dt=F32):
            return ctx.enter_context(nc.sbuf_tensor(name, shape, dt))

        def ps(name, shape):
            return ctx.enter_context(nc.psum_tensor(name, shape, F32))

        def sem(name):
            return ctx.enter_context(nc.semaphore(name))

        ids_sb = sb("ids_sb", [P, CHUNKS * GPC], I32)
        base_sb = sb("base_sb", [P, 1], I32)
        row_idx = sb("row_idx", [P, CHUNKS * GPC], I32)
        idx_now = sb("idx_now", [P, GPC], I32)
        ident = sb("ident", [P, P])
        rows = sb("rows", [P, GPC, DIM])
        e_t = sb("e_t", [P, 2, 2, KC, P])
        z = sb("z", [P, JJ, CHUNK])
        dense_sb = sb("dense_sb", [FIELDS, BATCH])
        w1_sb = sb("w1_sb", [P, JJ, HID1])
        w2_sb = sb("w2_sb", [P, N1, HID2])
        w3_sb = sb("w3_sb", [P, N2])
        b1_sb = sb("b1_sb", [P, N1])
        b2_sb = sb("b2_sb", [P, N2])
        h1 = sb("h1", [P, N1, CHUNK])
        h2 = sb("h2", [P, N2, CHUNK])
        y_sb = sb("y_sb", [1, BATCH])

        t_ps = ps("t_ps", [P, 2, 2, KC, P])
        g_ps = ps("g_ps", [P, 2, HALF, P])
        top_ps = ps("top_ps", [P, 2, 512])
        h1_acc = [top_ps[:, 2 * n // N1, n % (N1 // 2) * CHUNK:][:, :CHUNK] for n in range(N1)]
        h2_acc = [top_ps[:, n, 2 * CHUNK:3 * CHUNK] for n in range(N2)]
        y_acc = top_ps[0:1, 0, 3 * CHUNK:4 * CHUNK]

        ids_loaded = sem("ids_loaded")
        idx_first = sem("idx_first")
        idx_all = sem("idx_all")
        half_free = [sem("half_free0"), sem("half_free1")]
        ident_zeroed = sem("ident_zeroed")
        ident_ready = sem("ident_ready")
        w1_loaded = sem("w1_loaded")
        top_loaded = sem("top_loaded")
        gathered = [sem(f"gathered{s}") for s in range(GPC)]
        transposed = sem("transposed")
        e_dve = sem("e_dve")
        e_act = sem("e_act")
        grams = sem("grams")
        z_dve = sem("z_dve")
        z_act = sem("z_act")
        mm1 = sem("mm1")
        mm2 = sem("mm2")
        mm3 = sem("mm3")
        h1_ready = sem("h1_ready")
        h2_ready = sem("h2_ready")
        y_ready = sem("y_ready")
        stored = sem("stored")

        block = ctx.enter_context(nc.Block())

        @block.sync
        def _(sp):
            sp.dma_start(ids_sb[:], ids).then_inc(ids_loaded, 16)
            sp.dma_start(base_sb[:], row_base).then_inc(ids_loaded, 16)
            sp.dma_start(w1_sb[:], w1).then_inc(w1_loaded, 16)
            for dst, src in ((dense_sb, dense), (b1_sb, b1), (w2_sb, w2), (b2_sb, b2), (w3_sb, w3)):
                sp.dma_start(dst[:], src).then_inc(top_loaded, 16)
            sp.wait_ge(y_ready, CHUNKS)
            sp.dma_start(out, y_sb[:]).then_inc(stored, 16)
            sp.wait_ge(stored, 16)

        @block.gpsimd
        def _(pool):
            nc.gpsimd.memset(ident[:], 0.0).then_inc(ident_zeroed, 1)
            pool.wait_ge(ident_zeroed, 1)
            nc.gpsimd.affine_select(out=ident[:], in_=ident[:], compare_op=ALU.not_equal, fill=1.0,
                                    base=0, pattern=[[-1, P]], channel_multiplier=1).then_inc(ident_ready, 1)
            pool.wait_ge(idx_first, 1)

            def gather_chunk(c, first):
                for s in range(GPC):
                    if not first and s % HALF == 0:
                        pool.wait_ge(idx_first, 1)
                        pool.wait_ge(half_free[s // HALF], c)
                    nc.gpsimd.indirect_dma_start(
                        out=rows[:, s, :], out_offset=None, in_=tables,
                        in_offset=bass.IndirectOffsetOnAxis(ap=idx_now[:, s:s + 1], axis=0),
                    ).then_inc(gathered[s], 16)

            gather_chunk(0, True)
            with pool.Fori(1, CHUNKS) as c:
                gather_chunk(c, False)

        @block.tensor
        def _(pe):
            def transpose_pair(c, k, first):
                for g in range(2):
                    pe.wait_ge(gathered[2 * k + g], 16 * (c + 1))
                if not (first and k < 2):
                    pe.wait_ge(e_act if k % 2 else e_dve, c * (PAIRS // 2) + k // 2)
                for g in range(2):
                    for kc in range(KC):
                        last = nc.tensor.transpose(t_ps[:, k % 2, g, kc, :],
                                                   rows[:, 2 * k + g, kc * P:(kc + 1) * P], ident[:])
                last.then_inc(transposed, 1)

            def gram_pair(c, k, first):
                pe.wait_ge(e_act if k % 2 else e_dve, c * (PAIRS // 2) + k // 2 + 1)
                half = k // PPH
                if not first and k % PPH == 0:
                    pe.wait_ge(z_dve, (c - 1) * 2 + half + 1)
                    pe.wait_ge(z_act, (c - 1) * 2 + half + 1)
                for g in range(2):
                    for kc in range(KC):
                        e = e_t[:, k % 2, g, kc, :]
                        last = nc.tensor.matmul(g_ps[:, half, 2 * (k % PPH) + g, :], e, e,
                                                start=(kc == 0), stop=(kc == KC - 1))
                last.then_inc(grams, 1)

            def layer1(c, first):
                if first:
                    pe.wait_ge(w1_loaded, 16)
                pe.wait_ge(z_dve, 2 * (c + 1))
                pe.wait_ge(z_act, 2 * (c + 1))
                if not first:
                    pe.wait_ge(y_ready, c)
                for n in range(N1):
                    for jj in range(JJ):
                        last = nc.tensor.matmul(h1_acc[n], w1_sb[:, jj, n * P:(n + 1) * P], z[:, jj, :],
                                                start=(jj == 0), stop=(jj == JJ - 1))
                last.then_inc(mm1, 1)

            def layer2(c, first):
                if first:
                    pe.wait_ge(top_loaded, 16 * 5)
                pe.wait_ge(h1_ready, 2 * (c + 1))
                for n in range(N2):
                    for k in range(N1):
                        last = nc.tensor.matmul(h2_acc[n], w2_sb[:, k, n * P:(n + 1) * P], h1[:, k, :],
                                                start=(k == 0), stop=(k == N1 - 1))
                last.then_inc(mm2, 1)

            def layer3(c):
                pe.wait_ge(h2_ready, 2 * (c + 1))
                for k in range(N2):
                    last = nc.tensor.matmul(y_acc, w3_sb[:, k:k + 1], h2[:, k, :],
                                            start=(k == 0), stop=(k == N2 - 1))
                last.then_inc(mm3, 1)

            def chunk(c, first, second=False):
                for k in range(PAIRS):
                    transpose_pair(c, k, first)
                    if k > 0:
                        gram_pair(c, k - 1, first)
                    elif not first:
                        gram_pair(c - 1, PAIRS - 1, False)
                    if not first:
                        if k == 2:
                            layer1(c - 1, second)
                        elif k == 3:
                            layer2(c - 1, second)
                        elif k == 4:
                            layer3(c - 1)

            pe.wait_ge(ident_ready, 1)
            chunk(0, True)
            chunk(1, False, second=True)
            with pe.Fori(2, CHUNKS) as c:
                chunk(c, False)
            gram_pair(CHUNKS - 1, PAIRS - 1, False)
            layer1(CHUNKS - 1, False)
            layer2(CHUNKS - 1, False)
            layer3(CHUNKS - 1)

        def z_part(copy, half, quads):
            for sq in quads:
                for jq in range(JQ):
                    lo = 1 if jq == 0 else 0
                    col = sq * GPC + half * HALF
                    src = g_ps[FIELDS * sq:FIELDS * (sq + 1), half, :,
                               FIELDS * sq + JJ * jq + lo:FIELDS * sq + JJ * (jq + 1)]
                    dst = z[FIELDS * jq:FIELDS * (jq + 1), lo:JJ, col:col + HALF].rearrange("p j g -> p g j")
                    last = copy(dst, src)
            return last

        @block.vector
        def _(dve):
            dve.wait_ge(ids_loaded, 32)
            for dst, n, done in ((idx_now, GPC, idx_first), (row_idx, CHUNKS * GPC, idx_all)):
                nc.vector.tensor_tensor(dst[:], ids_sb[:, 0:n], base_sb[:, 0:1].to_broadcast([P, n]),
                                        ALU.add).then_inc(done, 1)

            def move_half(c, half):
                dve.wait_ge(grams, c * PAIRS + (half + 1) * PPH)
                z_part(nc.vector.tensor_copy, half, (0, 1)).then_inc(z_dve, 1)

            def keep_y(c):
                dve.wait_ge(mm3, c + 1)
                nc.vector.tensor_copy(y_sb[:, bass.ds(c * CHUNK, CHUNK)], y_acc).then_inc(y_ready, 1)

            def chunk(c, first, second=False):
                for k in range(PAIRS):
                    if k % 2 == 0:
                        dve.wait_ge(transposed, c * PAIRS + k + 1)
                        nc.vector.tensor_copy(e_t[:, 0], t_ps[:, 0]).then_inc(e_dve, 1)
                    if k == PPH:
                        if not first:
                            dve.wait_ge(mm1, c)
                        else:
                            dve.wait_ge(top_loaded, 16 * 5)
                        nc.vector.tensor_copy(z[0:FIELDS, 0, :], dense_sb[:, bass.ds(c * CHUNK, CHUNK)])
                        move_half(c, 0)
                    if not first:
                        if k == 0:
                            move_half(c - 1, 1)
                        elif k == 2:
                            relu1(c - 1)
                        elif k == 3:
                            relu2(c - 1)
                        elif k == 5:
                            keep_y(c - 1)

            def relu1(c):
                dve.wait_ge(mm1, c + 1)
                for n in range(N1 // 2):
                    last = nc.vector.tensor_scalar(h1[:, n, :], h1_acc[n], b1_sb[:, n:n + 1], 0.0,
                                                   ALU.add, ALU.max)
                last.then_inc(h1_ready, 1)

            def relu2(c):
                dve.wait_ge(mm2, c + 1)
                nc.vector.tensor_scalar(h2[:, 0, :], h2_acc[0], b2_sb[:, 0:1], 0.0,
                                        ALU.add, ALU.max).then_inc(h2_ready, 1)

            chunk(0, True)
            with dve.Fori(1, CHUNKS) as c:
                chunk(c, False)
            move_half(CHUNKS - 1, 1)
            relu1(CHUNKS - 1)
            relu2(CHUNKS - 1)
            keep_y(CHUNKS - 1)

        @block.scalar
        def _(act):
            def move_half(c, half):
                act.wait_ge(grams, c * PAIRS + (half + 1) * PPH)
                z_part(nc.scalar.copy, half, (2, 3)).then_inc(z_act, 1)

            def relu1(c):
                act.wait_ge(mm1, c + 1)
                for n in range(N1 // 2, N1):
                    last = nc.scalar.activation(h1[:, n, :], h1_acc[n], ACT.Relu, bias=b1_sb[:, n:n + 1])
                last.then_inc(h1_ready, 1)

            def relu2(c):
                act.wait_ge(mm2, c + 1)
                nc.scalar.activation(h2[:, 1, :], h2_acc[1], ACT.Relu,
                                     bias=b2_sb[:, 1:2]).then_inc(h2_ready, 1)

            def refresh(c, half):
                nc.scalar.copy(idx_now[:, half * HALF:(half + 1) * HALF],
                               row_idx[:, bass.ds(c * GPC + half * HALF, HALF)]).then_inc(half_free[half], 1)

            def chunk(c, first, last=False):
                for k in range(PAIRS):
                    if k == 0 and not first:
                        refresh(c, 1)
                    if k % 2 == 1:
                        act.wait_ge(transposed, c * PAIRS + k + 1)
                        nc.scalar.copy(e_t[:, 1], t_ps[:, 1]).then_inc(e_act, 1)
                    if k == PPH and not last:
                        refresh(c + 1, 0)
                    if k == PPH:
                        if not first:
                            act.wait_ge(mm1, c)
                        move_half(c, 0)
                    if not first:
                        if k == 0:
                            move_half(c - 1, 1)
                        elif k == 2:
                            relu1(c - 1)
                        elif k == 3:
                            relu2(c - 1)

            act.wait_ge(top_loaded, 16 * 5)
            act.wait_ge(idx_all, 1)
            chunk(0, True)
            with act.Fori(1, CHUNKS - 1) as c:
                chunk(c, False)
            chunk(CHUNKS - 1, False, last=True)
            move_half(CHUNKS - 1, 1)
            relu1(CHUNKS - 1)
            relu2(CHUNKS - 1)


def kernel(**inputs):
    import numpy as np
    import concourse.bacc as bacc
    from concourse.bass_utils import run_bass_kernel_spmd

    tables = [np.asarray(inputs[f"tbl_{f}"]) for f in range(FIELDS)]
    starts = np.concatenate([[0], np.cumsum([t.shape[0] for t in tables])[:-1]])
    ids = np.asarray(inputs["ids"]).reshape(CHUNKS, SPG, GPC, FIELDS).transpose(1, 3, 0, 2)
    w1 = np.asarray(inputs["W_top1"])
    pairs = FIELDS * (FIELDS - 1) // 2
    first, second = np.triu_indices(FIELDS, k=1)
    w1_z = np.zeros((JQ, FIELDS, JJ, HID1), w1.dtype)
    w1_z[second // JJ, first, second % JJ] = w1[:pairs]
    w1_z[0, :DENSE, 0] = w1[pairs:]
    dense = np.zeros((FIELDS, BATCH), np.asarray(inputs["dense_ctx"]).dtype)
    dense[:DENSE] = np.asarray(inputs["dense_ctx"]).T
    arrays = {
        "ids": np.ascontiguousarray(ids.reshape(P, CHUNKS * GPC)),
        "row_base": np.tile(starts.astype(np.int32), SPG).reshape(P, 1),
        "tables": np.concatenate(tables, axis=0),
        "dense": dense,
        "w1": w1_z.reshape(P, JJ, HID1),
        "b1": np.ascontiguousarray(np.asarray(inputs["b_top1"]).reshape(N1, P).T),
        "w2": np.ascontiguousarray(np.asarray(inputs["W_top2"]).reshape(N1, P, HID2).transpose(1, 0, 2)),
        "b2": np.ascontiguousarray(np.asarray(inputs["b_top2"]).reshape(N2, P).T),
        "w3": np.ascontiguousarray(np.asarray(inputs["W_top3"]).reshape(N2, P).T),
    }
    nc = bacc.Bacc("TRN2", target_bir_lowering=False, num_devices=1)
    args = [nc.dram_tensor(name, a.shape, mybir.dt.from_np(a.dtype), kind="ExternalInput").ap()
            for name, a in arrays.items()]
    out = nc.dram_tensor("y", (1, BATCH), F32, kind="ExternalOutput").ap()
    dlrm_tower(nc, *args, out)
    result = run_bass_kernel_spmd(nc, [arrays], core_ids=[0])
    return result.results[0]["y"].reshape(BATCH, 1)
```

```python
from contextlib import ExitStack

import concourse.bass as bass
from concourse import mybir

F32 = mybir.dt.float32
I32 = mybir.dt.int32
ALU = mybir.AluOpType
ACT = mybir.ActivationFunctionType

P = 128
BATCH = 512
FIELDS = 32
DIM = 256
DENSE = 16
HID1 = 512
HID2 = 256
KC = DIM // P
SPG = P // FIELDS
SLOTS = 16
GPQ = 8
QS = GPQ * SPG
QUARTERS = 4
BLOCK = QUARTERS * QS
BLOCKS = BATCH // BLOCK
GROUPS = BATCH // SPG
PPQ = GPQ // 2
PAIRS = QUARTERS * PPQ
ROUNDS = GROUPS // SLOTS
JQ = P // FIELDS
JJ = FIELDS // JQ
N1 = HID1 // P
N2 = HID2 // P
WARM = 10
L1, L2, L3 = 1, 6, 8
LAST_L1 = {9: 0, 11: 1, 14: 2}
LAST_TURN = {10: 0, 12: 1, 15: 2}


def dlrm_tower(nc, ids, tables, dense, w1, w2, b2, w3, out):
    ctx = ExitStack()
    with ctx:
        def sb(name, shape, dt=F32):
            return ctx.enter_context(nc.sbuf_tensor(name, shape, dt))

        def ps(name, shape):
            return ctx.enter_context(nc.psum_tensor(name, shape, F32))

        def sem(name):
            return ctx.enter_context(nc.semaphore(name))

        ids_sb = sb("ids_sb", [P, GROUPS + 1], I32)
        row_idx = sb("row_idx", [P, GROUPS], I32)
        idx_now = sb("idx_now", [P, SLOTS], I32)
        ident = sb("ident", [P, P])
        rows = sb("rows", [P, SLOTS, DIM])
        e_t = sb("e_t", [P, 2, 2, KC, P])
        z = sb("z", [P, JJ, BLOCK])
        dense_sb = sb("dense_sb", [FIELDS, BATCH])
        w1_sb = sb("w1_sb", [P, JJ, HID1])
        w2_sb = sb("w2_sb", [P, N1, HID2])
        w3_sb = sb("w3_sb", [P, N2])
        b2_sb = sb("b2_sb", [P, N2])
        h1_s = sb("h1_s", [P, P])
        h1 = sb("h1", [P, N1, BLOCK])
        h2 = sb("h2", [P, N2, BLOCK])
        y_sb = sb("y_sb", [1, BATCH])

        t_ps = ps("t_ps", [P, 2, 2, KC, P])
        g_ps = ps("g_ps", [P, 2, GPQ, P])
        dve_ps = ps("dve_ps", [P, 512])
        act_ps = ps("act_ps", [P, 512])
        h1_dve = dve_ps[:, 0:N1 // 2 * BLOCK]
        h1_act = act_ps[:, 0:N1 // 2 * BLOCK]
        h1_acc = [ps_[:, n * BLOCK:(n + 1) * BLOCK] for ps_ in (h1_dve, h1_act) for n in range(N1 // 2)]
        h2_acc = [ps_[:, N1 // 2 * BLOCK:][:, :BLOCK] for ps_ in (dve_ps, act_ps)]
        y_acc = dve_ps[0:1, (N1 // 2 + 1) * BLOCK:][:, :BLOCK]
        quarter_acc = dve_ps[:, 0:P]
        turned_acc = act_ps[:, 0:P]

        ids_loaded = sem("ids_loaded")
        idx_first = sem("idx_first")
        idx_all = sem("idx_all")
        half_free = [sem("half_free0"), sem("half_free1")]
        ident_zeroed = sem("ident_zeroed")
        ident_ready = sem("ident_ready")
        dense_loaded = sem("dense_loaded")
        w1_loaded = sem("w1_loaded")
        top_loaded = sem("top_loaded")
        gathered = [sem(f"gathered{s}") for s in range(SLOTS)]
        transposed = sem("transposed")
        e_dve = sem("e_dve")
        e_act = sem("e_act")
        grams = sem("grams")
        z_dve = sem("z_dve")
        z_act = sem("z_act")
        mm1_dve = sem("mm1_dve")
        mm1_act = sem("mm1_act")
        relu1_dve = sem("relu1_dve")
        relu1_act = sem("relu1_act")
        mm1_quarter = sem("mm1_quarter")
        relu1_quarter = sem("relu1_quarter")
        turned = sem("turned")
        h1_kept = sem("h1_kept")
        mm2 = sem("mm2")
        h2_dve = sem("h2_dve")
        h2_act = sem("h2_act")
        mm3 = sem("mm3")
        y_ready = sem("y_ready")
        stored = sem("stored")

        block = ctx.enter_context(nc.Block())

        @block.sync
        def _(sp):
            sp.dma_start(ids_sb[:], ids).then_inc(ids_loaded, 16)
            sp.dma_start(dense_sb[:], dense).then_inc(dense_loaded, 16)
            for jj in range(JJ):
                sp.wait_ge(gathered[jj], 16)
                sp.dma_start(w1_sb[:, jj], w1[:, jj]).then_inc(w1_loaded, 16)
            for dst, src in ((w2_sb, w2), (b2_sb, b2), (w3_sb, w3)):
                sp.dma_start(dst[:], src).then_inc(top_loaded, 16)
            sp.wait_ge(y_ready, BLOCKS)
            sp.dma_start(out, y_sb[:]).then_inc(stored, 16)
            sp.wait_ge(stored, 16)

        @block.gpsimd
        def _(pool):
            nc.gpsimd.memset(ident[:], 0.0).then_inc(ident_zeroed, 1)
            pool.wait_ge(ident_zeroed, 1)
            nc.gpsimd.affine_select(out=ident[:], in_=ident[:], compare_op=ALU.not_equal, fill=1.0,
                                    base=0, pattern=[[-1, P]], channel_multiplier=1).then_inc(ident_ready, 1)
            pool.wait_ge(idx_first, 1)

            def gather(s):
                nc.gpsimd.indirect_dma_start(
                    out=rows[:, s, :], out_offset=None, in_=tables,
                    in_offset=bass.IndirectOffsetOnAxis(ap=idx_now[:, s:s + 1], axis=0),
                ).then_inc(gathered[s], 16)

            for s in range(SLOTS):
                gather(s)
            with pool.Fori(1, ROUNDS) as r:
                for s in range(SLOTS):
                    if s % (SLOTS // 2) == 0:
                        pool.wait_ge(idx_first, 1)
                        pool.wait_ge(half_free[s // (SLOTS // 2)], r)
                    gather(s)

        @block.tensor
        def _(pe):
            def transpose_pair(b, k):
                for g in range(2):
                    s = 2 * k + g
                    pe.wait_ge(gathered[s % SLOTS], 16 * (b * (2 * PAIRS // SLOTS) + s // SLOTS + 1))
                    for i in range(KC):
                        last = nc.tensor.transpose(t_ps[:, k % 2, g, i], rows[:, s % SLOTS, i * P:(i + 1) * P],
                                                   ident[:])
                last.then_inc(transposed, 1)

            def gram_pair(b, k, first=False, tiled=False):
                pe.wait_ge(e_act if k % 2 else e_dve, b * (PAIRS // 2) + k // 2 + 1)
                quarter = k // PPQ
                if k % PPQ == 0 and not (first and quarter < 2):
                    pe.wait_ge(z_dve, b * QUARTERS + quarter - 1)
                    pe.wait_ge(z_act, b * QUARTERS + quarter - 1)
                for g in range(2):
                    acc = g_ps[:, quarter % 2, 2 * (k % PPQ) + g]
                    for i in range(KC):
                        e = e_t[:, k % 2, g, i]
                        lanes = [slice(q * FIELDS, (q + 1) * FIELDS) for q in range(SPG)] if tiled else [slice(0, P)]
                        for lane in lanes:
                            last = nc.tensor.matmul(acc[lane, lane], e[:, lane], e[:, lane],
                                                    start=(i == 0), stop=(i == KC - 1))
                if k % PPQ == PPQ - 1:
                    last.then_inc(grams, 1)

            def layer1(b, n, after_first):
                if n == 0:
                    pe.wait_ge(z_dve, QUARTERS * (b + 1))
                    pe.wait_ge(z_act, QUARTERS * (b + 1))
                    if after_first:
                        pe.wait_ge(y_ready, b)
                for jj in range(JJ):
                    last = nc.tensor.matmul(h1_acc[n], w1_sb[:, jj, n * P:(n + 1) * P], z[:, jj],
                                            start=(jj == 0), stop=(jj == JJ - 1))
                if n == N1 // 2 - 1:
                    last.then_inc(mm1_dve, 1)
                elif n == N1 - 1:
                    last.then_inc(mm1_act, 1)

            def layer2():
                for n in range(N2):
                    for i in range(N1):
                        last = nc.tensor.matmul(h2_acc[n], w2_sb[:, i, n * P:(n + 1) * P], h1[:, i],
                                                start=(i == 0), stop=(i == N1 - 1))
                last.then_inc(mm2, 1)

            def layer3(b):
                pe.wait_ge(h2_dve, b + 1)
                pe.wait_ge(h2_act, b + 1)
                for i in range(N2):
                    last = nc.tensor.matmul(y_acc, w3_sb[:, i:i + 1], h2[:, i],
                                            start=(i == 0), stop=(i == N2 - 1))
                last.then_inc(mm3, 1)

            def network(b, k, after_first):
                if L1 <= k < L1 + N1:
                    layer1(b, k - L1, after_first)
                elif k == L2:
                    pe.wait_ge(relu1_dve, b + 1)
                    pe.wait_ge(relu1_act, b + 1)
                    layer2()
                elif k == L3:
                    layer3(b)

            def layer1_quarter(q):
                pe.wait_ge(z_dve, (BLOCKS - 1) * QUARTERS + q + 1)
                pe.wait_ge(z_act, (BLOCKS - 1) * QUARTERS + q + 1)
                if q == 0:
                    pe.wait_ge(y_ready, BLOCKS - 1)
                for jj in range(JJ):
                    for n in range(N1):
                        last = nc.tensor.matmul(quarter_acc[n * QS:(n + 1) * QS], z[:, jj, q * QS:(q + 1) * QS],
                                                w1_sb[:, jj, n * P:(n + 1) * P],
                                                start=(jj == 0), stop=(jj == JJ - 1))
                last.then_inc(mm1_quarter, 1)

            def turn_quarter(q):
                pe.wait_ge(relu1_quarter, q + 1)
                if q > 0:
                    pe.wait_ge(h1_kept, q)
                nc.tensor.transpose(turned_acc, h1_s[:], ident[:]).then_inc(turned, 1)

            pe.wait_ge(ident_ready, 1)
            for _ in range(WARM):
                nc.tensor.matmul(dve_ps[:, 0:P], ident[:], ident[:], start=True, stop=True)
            for k in range(PAIRS):
                transpose_pair(0, k)
                if k > 0:
                    gram_pair(0, k - 1, first=True)
            pe.wait_ge(w1_loaded, 16 * JJ)
            pe.wait_ge(top_loaded, 16 * 3)
            with pe.Fori(1, BLOCKS - 1) as b:
                for k in range(PAIRS):
                    transpose_pair(b, k)
                    if L1 <= k < L1 + N1:
                        network(b - 1, k, False)
                    gram_pair(b, k - 1) if k else gram_pair(b - 1, PAIRS - 1)
                    if k >= L1 + N1:
                        network(b - 1, k, False)
            last_b = BLOCKS - 1
            for k in range(PAIRS):
                transpose_pair(last_b, k)
                if L1 <= k < L1 + N1:
                    network(last_b - 1, k, True)
                gram_pair(last_b, k - 1, tiled=True) if k else gram_pair(last_b - 1, PAIRS - 1)
                if k >= L1 + N1:
                    network(last_b - 1, k, True)
                if k in LAST_L1:
                    layer1_quarter(LAST_L1[k])
                elif k in LAST_TURN:
                    turn_quarter(LAST_TURN[k])
            gram_pair(last_b, PAIRS - 1, tiled=True)
            layer1_quarter(QUARTERS - 1)
            turn_quarter(QUARTERS - 1)
            pe.wait_ge(h1_kept, QUARTERS)
            layer2()
            layer3(last_b)

        def move(copy, quarter, sample_quads):
            for sq in sample_quads:
                for jq in range(JQ):
                    lo = 1 if jq == 0 else 0
                    col = FIELDS * sq + JJ * jq
                    src = g_ps[FIELDS * sq:FIELDS * (sq + 1), quarter % 2, :, col + lo:col + JJ]
                    at = quarter * QS + sq * GPQ
                    dst = z[FIELDS * jq:FIELDS * (jq + 1), lo:JJ, at:at + GPQ]
                    last = copy(dst.rearrange("p j g -> p g j"), src)
            return last

        @block.vector
        def _(dve):
            dve.wait_ge(ids_loaded, 16)
            for dst, n, done in ((idx_now, SLOTS, idx_first), (row_idx, GROUPS, idx_all)):
                nc.vector.tensor_tensor(dst[:], ids_sb[:, 0:n], ids_sb[:, GROUPS:].to_broadcast([P, n]),
                                        ALU.add).then_inc(done, 1)

            def copy_pair(b, k):
                dve.wait_ge(transposed, b * PAIRS + k + 1)
                nc.vector.tensor_copy(e_t[:, k % 2], t_ps[:, k % 2]).then_inc(e_dve, 1)

            def move_quarter(b, q):
                dve.wait_ge(grams, b * QUARTERS + q + 1)
                move(nc.vector.tensor_copy, q, range(SPG // 2)).then_inc(z_dve, 1)

            def relu1(b):
                dve.wait_ge(mm1_dve, b + 1)
                nc.vector.tensor_scalar(h1[:, 0:N1 // 2], h1_dve.rearrange("p (n s) -> p n s", s=BLOCK), 0.0, None,
                                        ALU.max).then_inc(relu1_dve, 1)

            def relu2(b):
                dve.wait_ge(mm2, b + 1)
                nc.vector.tensor_scalar(h2[:, 0], h2_acc[0], b2_sb[:, 0:1], 0.0,
                                        ALU.add, ALU.max).then_inc(h2_dve, 1)

            def keep_y(b):
                dve.wait_ge(mm3, b + 1)
                nc.vector.tensor_copy(y_sb[:, bass.ds(b * BLOCK, BLOCK)], y_acc).then_inc(y_ready, 1)

            def relu1_of_quarter(q):
                dve.wait_ge(mm1_quarter, q + 1)
                nc.vector.tensor_scalar(h1_s[:], quarter_acc, 0.0, None, ALU.max).then_inc(relu1_quarter, 1)

            def run(b, has_last_block, is_last=False):
                for k in range(0, PAIRS, 2):
                    copy_pair(b, k)
                    if has_last_block:
                        if k == 0:
                            move_quarter(b - 1, QUARTERS - 1)
                        elif k == 2:
                            relu1(b - 1)
                        elif k == L2:
                            relu2(b - 1)
                        elif k == L3:
                            keep_y(b - 1)
                    if k > 0 and k % PPQ == 0:
                        move_quarter(b, k // PPQ - 1)
                    if is_last:
                        for step in (k, k + 1):
                            if step in LAST_L1:
                                relu1_of_quarter(LAST_L1[step])

            run(0, False)
            dve.wait_ge(top_loaded, 16 * 3)
            with dve.Fori(1, BLOCKS - 1) as b:
                run(b, True)
            last_b = BLOCKS - 1
            run(last_b, True, is_last=True)
            move_quarter(last_b, QUARTERS - 1)
            relu1_of_quarter(QUARTERS - 1)
            relu2(last_b)
            keep_y(last_b)

        @block.scalar
        def _(act):
            def copy_pair(b, k):
                act.wait_ge(transposed, b * PAIRS + k + 1)
                nc.scalar.copy(e_t[:, k % 2], t_ps[:, k % 2]).then_inc(e_act, 1)

            def move_quarter(b, q):
                act.wait_ge(grams, b * QUARTERS + q + 1)
                nc.scalar.copy(z[0:FIELDS, 0, q * QS:(q + 1) * QS],
                               dense_sb[:, bass.ds(b * BLOCK + q * QS, QS)])
                move(nc.scalar.copy, q, range(SPG // 2, SPG)).then_inc(z_act, 1)

            def relu1(b):
                act.wait_ge(mm1_act, b + 1)
                nc.scalar.activation(h1[:, N1 // 2:], h1_act.rearrange("p (n s) -> p n s", s=BLOCK),
                                     ACT.Relu).then_inc(relu1_act, 1)

            def relu2(b):
                act.wait_ge(mm2, b + 1)
                nc.scalar.activation(h2[:, 1], h2_acc[1], ACT.Relu, bias=b2_sb[:, 1:2]).then_inc(h2_act, 1)

            def keep_h1(q):
                act.wait_ge(turned, q + 1)
                nc.scalar.copy(h1[:, :, q * QS:(q + 1) * QS],
                               turned_acc.rearrange("p (n s) -> p n s", n=N1)).then_inc(h1_kept, 1)

            def refresh(b, q):
                nc.scalar.copy(idx_now[:, q % 2 * GPQ:(q % 2 + 1) * GPQ],
                               row_idx[:, bass.ds(b * QUARTERS * GPQ + (q + 2) * GPQ, GPQ)]
                               ).then_inc(half_free[q % 2], 1)

            def run(b, has_last_block, is_last=False):
                for k in range(1, PAIRS, 2):
                    copy_pair(b, k)
                    if k % PPQ == PPQ - 1 and not (is_last and k // PPQ >= QUARTERS - 2):
                        refresh(b, k // PPQ)
                    if has_last_block:
                        if k == 1:
                            move_quarter(b - 1, QUARTERS - 1)
                        elif k == L1 + N1:
                            relu1(b - 1)
                        elif k == L2 + 1:
                            relu2(b - 1)
                    if k > PPQ and k % PPQ == 1:
                        move_quarter(b, k // PPQ - 1)
                    if is_last:
                        for step in (k, k + 1):
                            if step in LAST_TURN:
                                keep_h1(LAST_TURN[step])

            act.wait_ge(dense_loaded, 16)
            act.wait_ge(idx_all, 1)
            run(0, False)
            act.wait_ge(top_loaded, 16 * 3)
            with act.Fori(1, BLOCKS - 1) as b:
                run(b, True)
            last_b = BLOCKS - 1
            run(last_b, True, is_last=True)
            move_quarter(last_b, QUARTERS - 1)
            keep_h1(QUARTERS - 1)
            relu2(last_b)


def kernel(**inputs):
    import numpy as np
    import concourse.bacc as bacc
    from concourse.bass_utils import run_bass_kernel_spmd

    tables = [np.asarray(inputs[f"tbl_{f}"]) for f in range(FIELDS)]
    starts = np.concatenate([[0], np.cumsum([t.shape[0] for t in tables])[:-1]]).astype(np.int32)
    ids = np.asarray(inputs["ids"]).reshape(BATCH // QS, SPG, GPQ, FIELDS).transpose(1, 3, 0, 2)
    ids = np.concatenate([ids.reshape(P, GROUPS), np.tile(starts, SPG).reshape(P, 1)], axis=1)
    w1 = np.asarray(inputs["W_top1"])
    pairs = FIELDS * (FIELDS - 1) // 2
    first, second = np.triu_indices(FIELDS, k=1)
    w1_z = np.zeros((JQ, FIELDS, JJ, HID1), w1.dtype)
    w1_z[second // JJ, first, second % JJ] = w1[:pairs]
    w1_z[0, :DENSE, 0] = w1[pairs:]
    w1_z[0, DENSE, 0] = np.asarray(inputs["b_top1"])
    dense = np.zeros((FIELDS, BATCH), np.asarray(inputs["dense_ctx"]).dtype)
    dense[:DENSE] = np.asarray(inputs["dense_ctx"]).T
    dense[DENSE] = 1.0
    arrays = {
        "ids": ids,
        "tables": np.concatenate(tables, axis=0),
        "dense": dense,
        "w1": w1_z.reshape(P, JJ, HID1),
        "w2": np.ascontiguousarray(np.asarray(inputs["W_top2"]).reshape(N1, P, HID2).transpose(1, 0, 2)),
        "b2": np.ascontiguousarray(np.asarray(inputs["b_top2"]).reshape(N2, P).T),
        "w3": np.ascontiguousarray(np.asarray(inputs["W_top3"]).reshape(N2, P).T),
    }
    nc = bacc.Bacc("TRN2", target_bir_lowering=False, num_devices=1)
    args = [nc.dram_tensor(name, a.shape, mybir.dt.from_np(a.dtype), kind="ExternalInput").ap()
            for name, a in arrays.items()]
    out = nc.dram_tensor("y", (1, BATCH), F32, kind="ExternalOutput").ap()
    dlrm_tower(nc, *args, out)
    result = run_bass_kernel_spmd(nc, [arrays], core_ids=[0])
    return result.results[0]["y"].reshape(BATCH, 1)
```

```python
from contextlib import ExitStack

import concourse.bass as bass
from concourse import mybir

F32 = mybir.dt.float32
I32 = mybir.dt.int32
ALU = mybir.AluOpType
ACT = mybir.ActivationFunctionType

P = 128
BATCH = 512
FIELDS = 32
DIM = 256
DENSE = 16
HID1 = 512
HID2 = 256
KC = DIM // P
SPG = P // FIELDS
GPQ = 8
QS = GPQ * SPG
QUARTERS = 4
BLOCK = QUARTERS * QS
BLOCKS = BATCH // BLOCK
GROUPS = BATCH // SPG
SLOTS = QUARTERS * GPQ
PPQ = GPQ // 2
PAIRS = QUARTERS * PPQ
JQ = P // FIELDS
JJ = FIELDS // JQ
N1 = HID1 // P
N2 = HID2 // P
WARM = 10
NEXT_L1, NEXT_TURN, L2, L3 = 1, 3, 4, 6
OWN_L1, OWN_TURN = 9, 11
LAST_L1, LAST_TURN = (7, 9, 13), (8, 11, 14)
GRAM_FIRST = 13
LAST_PIECES = 2 * (BLOCKS - 1)
EARLY = BLOCK - QS
TU = HID2 // SPG


def dlrm_tower(nc, ids, tables, dense, w1, w2, b2, w3, tail, out):
    ctx = ExitStack()
    with ctx:
        def sb(name, shape, dt=F32):
            return ctx.enter_context(nc.sbuf_tensor(name, shape, dt))

        def ps(name, shape):
            return ctx.enter_context(nc.psum_tensor(name, shape, F32))

        def sem(name):
            return ctx.enter_context(nc.semaphore(name))

        ids_sb = sb("ids_sb", [P, GROUPS + 1], I32)
        row_idx = sb("row_idx", [P, GROUPS], I32)
        idx_now = sb("idx_now", [P, SLOTS], I32)
        ident = sb("ident", [P, P])
        rows = sb("rows", [P, SLOTS, DIM])
        e_t = sb("e_t", [P, 2, 2, KC, P])
        z = sb("z", [P, JJ, BLOCK])
        dense_sb = sb("dense_sb", [FIELDS, BATCH])
        w1_sb = sb("w1_sb", [P, JJ, HID1])
        w2_sb = sb("w2_sb", [P, N1, HID2])
        w3_sb = sb("w3_sb", [P, N2])
        b2_sb = sb("b2_sb", [P, N2])
        h1_s = sb("h1_s", [P, HID1 // 2])
        h1 = sb("h1", [P, N1, BLOCK])
        h2 = sb("h2", [P, N2, BLOCK])
        y_sb = sb("y_sb", [1, BATCH])
        tail_sb = sb("tail_sb", [P, HID2 + 2 * QS + TU])
        b2_row = tail_sb[:, 0:HID2]
        one_row = tail_sb[:, HID2:HID2 + QS]
        tile_sum = tail_sb[:, HID2 + QS:HID2 + 2 * QS]
        w3_tile = tail_sb[:, HID2 + 2 * QS:]
        h2_w3 = sb("h2_w3", [P, TU])
        y_part = sb("y_part", [P, 1])

        t_ps = ps("t_ps", [P, 2, 2, KC, P])
        g_ps = ps("g_ps", [P, 2, GPQ, P])
        dve_ps = ps("dve_ps", [P, 512])
        act_ps = ps("act_ps", [P, 512])
        h1_acc = dve_ps[:, 0:HID1 // 2]
        turned_acc = act_ps[:, 0:HID1 // 2]
        h2_acc = [ps_[:, HID1 // 2:][:, :BLOCK] for ps_ in (dve_ps, act_ps)]
        y_acc = dve_ps[0:1, HID1 // 2 + BLOCK:][:, :BLOCK]
        h2_early = [g_ps[:, 0, n * GPQ // 2, 0:EARLY] for n in range(2)]
        y_early = g_ps[0:1, 0, 1, 0:EARLY]
        h2_last = t_ps[:, 0, 0, 0, 0:TU]
        y_last = t_ps[0:1, 1, 0, 0, 0:QS]

        ids_loaded = sem("ids_loaded")
        idx_first = sem("idx_first")
        idx_all = sem("idx_all")
        slots_free = [sem(f"slots_free{q}") for q in range(QUARTERS)]
        ident_zeroed = sem("ident_zeroed")
        ident_ready = sem("ident_ready")
        dense_loaded = sem("dense_loaded")
        w1_loaded = sem("w1_loaded")
        top_loaded = sem("top_loaded")
        gathered = [sem(f"gathered{s}") for s in range(SLOTS)]
        transposed = sem("transposed")
        e_dve = sem("e_dve")
        e_act = sem("e_act")
        grams = sem("grams")
        z_dve = sem("z_dve")
        z_act = sem("z_act")
        mm1 = sem("mm1")
        relu1 = sem("relu1")
        turned = sem("turned")
        h1_kept = sem("h1_kept")
        mm2 = sem("mm2")
        h2_dve = sem("h2_dve")
        h2_act = sem("h2_act")
        mm3 = sem("mm3")
        y_ready = sem("y_ready")
        e_last = sem("e_last")
        grams_half = sem("grams_half")
        mm2_early = sem("mm2_early")
        h2_early_dve = sem("h2_early_dve")
        h2_early_act = sem("h2_early_act")
        mm3_early = sem("mm3_early")
        y_early_ready = sem("y_early_ready")
        mm2_last = sem("mm2_last")
        y_part_ready = sem("y_part_ready")
        stored = sem("stored")

        block = ctx.enter_context(nc.Block())

        @block.sync
        def _(sp):
            sp.dma_start(ids_sb[:], ids).then_inc(ids_loaded, 16)
            sp.dma_start(dense_sb[:], dense).then_inc(dense_loaded, 16)
            for jj in range(JJ):
                sp.wait_ge(gathered[jj], 16)
                sp.dma_start(w1_sb[:, jj], w1[:, jj]).then_inc(w1_loaded, 16)
            for dst, src in ((w2_sb, w2), (b2_sb, b2), (w3_sb, w3), (tail_sb, tail)):
                sp.dma_start(dst[:], src).then_inc(top_loaded, 16)
            sp.wait_ge(y_early_ready, 1)
            sp.wait_ge(y_ready, BLOCKS)
            sp.dma_start(out, y_sb[:]).then_inc(stored, 16)
            sp.wait_ge(stored, 16)

        @block.gpsimd
        def _(pool):
            nc.gpsimd.memset(ident[:], 0.0).then_inc(ident_zeroed, 1)
            pool.wait_ge(ident_zeroed, 1)
            nc.gpsimd.affine_select(out=ident[:], in_=ident[:], compare_op=ALU.not_equal, fill=1.0,
                                    base=0, pattern=[[-1, P]], channel_multiplier=1).then_inc(ident_ready, 1)
            pool.wait_ge(idx_first, 1)

            def gather(s):
                nc.gpsimd.indirect_dma_start(
                    out=rows[:, s, :], out_offset=None, in_=tables,
                    in_offset=bass.IndirectOffsetOnAxis(ap=idx_now[:, s:s + 1], axis=0),
                ).then_inc(gathered[s], 16)

            for s in range(SLOTS):
                gather(s)
            with pool.Fori(1, BLOCKS) as b:
                for s in range(SLOTS):
                    if s % GPQ == 0:
                        pool.wait_ge(idx_first, 1)
                        pool.wait_ge(slots_free[s // GPQ], b)
                    gather(s)

        @block.tensor
        def _(pe):
            def transpose_group(b, s, pair):
                pe.wait_ge(gathered[s], 16 * (b + 1))
                for i in range(KC):
                    last = nc.tensor.transpose(t_ps[:, pair, s % 2, i], rows[:, s, i * P:(i + 1) * P], ident[:])
                return last

            def transpose_pair(b, k):
                transpose_group(b, 2 * k, k % 2)
                transpose_group(b, 2 * k + 1, k % 2).then_inc(transposed, 1)

            def tiled_gram(s, pair):
                acc = g_ps[:, s // GPQ % 2, s % GPQ]
                for i in range(KC):
                    e = e_t[:, pair, s % 2, i]
                    for q in range(SPG):
                        lane = slice(q * FIELDS, (q + 1) * FIELDS)
                        last = nc.tensor.matmul(acc[lane, lane], e[:, lane], e[:, lane],
                                                start=(i == 0), stop=(i == KC - 1))
                return last

            def gram_pair(b, k, first=False, tiled=False):
                pe.wait_ge(e_act if k % 2 else e_dve, b * (PAIRS // 2) + k // 2 + 1)
                quarter = k // PPQ
                if k % PPQ == 0 and not (first and quarter < 2):
                    pe.wait_ge(z_dve, b * QUARTERS + quarter - 1)
                    pe.wait_ge(z_act, b * QUARTERS + quarter - 1)
                for s in (2 * k, 2 * k + 1):
                    if tiled:
                        last = tiled_gram(s, k % 2)
                        continue
                    for i in range(KC):
                        e = e_t[:, k % 2, s % 2, i]
                        last = nc.tensor.matmul(g_ps[:, quarter % 2, s % GPQ], e, e,
                                                start=(i == 0), stop=(i == KC - 1))
                if k % PPQ == PPQ - 1:
                    last.then_inc(grams, 1)
                elif tiled and k == PAIRS - 3:
                    last.then_inc(grams_half, 1)

            def layer1(tiles, at, samples):
                units = HID1 // tiles
                for jj in range(JJ):
                    for t in range(tiles):
                        last = nc.tensor.matmul(h1_acc[t * samples:(t + 1) * samples, 0:units],
                                                z[:, jj, at:at + samples],
                                                w1_sb[:, jj, t * units:(t + 1) * units],
                                                start=(jj == 0), stop=(jj == JJ - 1))
                last.then_inc(mm1, 1)

            def piece(b, half):
                pe.wait_ge(z_dve, QUARTERS * b + 2 * (half + 1))
                pe.wait_ge(z_act, QUARTERS * b + 2 * (half + 1))
                layer1(2, half * 2 * QS, 2 * QS)

            def quarter_piece(q):
                pe.wait_ge(z_dve, QUARTERS * (BLOCKS - 1) + q + 1)
                pe.wait_ge(z_act, QUARTERS * (BLOCKS - 1) + q + 1)
                layer1(SPG, q * QS, QS)

            def turn(p, first=False, units=HID1 // 2):
                pe.wait_ge(relu1, p + 1)
                if not first:
                    pe.wait_ge(h1_kept, p)
                for u in range(0, units, P):
                    last = nc.tensor.transpose(turned_acc[:, u:u + P], h1_s[:, u:u + P], ident[:])
                last.then_inc(turned, 1)

            def layer2():
                for n in range(N2):
                    for i in range(N1):
                        last = nc.tensor.matmul(h2_acc[n], w2_sb[:, i, n * P:(n + 1) * P], h1[:, i],
                                                start=(i == 0), stop=(i == N1 - 1))
                last.then_inc(mm2, 1)

            def layer3(b):
                pe.wait_ge(h2_dve, b + 1)
                pe.wait_ge(h2_act, b + 1)
                for i in range(N2):
                    last = nc.tensor.matmul(y_acc, w3_sb[:, i:i + 1], h2[:, i],
                                            start=(i == 0), stop=(i == N2 - 1))
                last.then_inc(mm3, 1)

            def network(b, k, first=False, is_last=False):
                if not first:
                    if k == NEXT_L1:
                        piece(b - 1, 1)
                    elif k == NEXT_TURN:
                        turn(2 * b - 1)
                    elif k == L2:
                        pe.wait_ge(h1_kept, 2 * b)
                        layer2()
                    elif k == L3:
                        layer3(b - 1)
                if is_last:
                    for q in range(QUARTERS - 1):
                        if k == LAST_L1[q]:
                            pe.wait_ge(y_ready, b)
                            quarter_piece(q)
                        elif k == LAST_TURN[q]:
                            turn(LAST_PIECES + q, units=P)
                elif k == OWN_L1:
                    if not first:
                        pe.wait_ge(y_ready, b)
                    piece(b, 0)
                elif k == OWN_TURN:
                    turn(2 * b, first)

            def layer2_early(n, parts):
                for i in parts:
                    last = nc.tensor.matmul(h2_early[n], w2_sb[:, i, n * P:(n + 1) * P], h1[:, i, 0:EARLY],
                                            start=(i == 0), stop=(i == N1 - 1))
                if i == N1 - 1:
                    last.then_inc(mm2_early, 1)

            def layer2_last():
                for t in range(SPG):
                    nc.tensor.matmul(h2_last[t * QS:(t + 1) * QS], one_row, b2_row[:, t * TU:(t + 1) * TU],
                                     start=True, stop=False)
                for i in range(N1):
                    for t in range(SPG):
                        last = nc.tensor.matmul(h2_last[t * QS:(t + 1) * QS], h1[:, i, EARLY:],
                                                w2_sb[:, i, t * TU:(t + 1) * TU], start=False, stop=(i == N1 - 1))
                last.then_inc(mm2_last, 1)

            pe.wait_ge(ident_ready, 1)
            for _ in range(WARM):
                nc.tensor.matmul(dve_ps[:, 0:P], ident[:], ident[:], start=True, stop=True)
            for k in range(PAIRS):
                transpose_pair(0, k)
                if k > 0:
                    gram_pair(0, k - 1, first=True)
                if k == OWN_L1:
                    pe.wait_ge(w1_loaded, 16 * JJ)
                network(0, k, first=True)
            pe.wait_ge(top_loaded, 16 * 4)
            with pe.Fori(1, BLOCKS - 1) as b:
                for k in range(PAIRS):
                    transpose_pair(b, k)
                    gram_pair(b, k - 1) if k else gram_pair(b - 1, PAIRS - 1)
                    network(b, k)
            last_b = BLOCKS - 1
            for k in range(PAIRS - 1):
                if k == GRAM_FIRST:
                    gram_pair(last_b, k - 1, tiled=True)
                transpose_pair(last_b, k)
                if k == 0:
                    gram_pair(last_b - 1, PAIRS - 1)
                elif k != GRAM_FIRST:
                    gram_pair(last_b, k - 1, tiled=True)
                network(last_b, k, is_last=True)
            transpose_group(last_b, SLOTS - 2, 1).then_inc(transposed, 1)
            pe.wait_ge(e_dve, BLOCKS * PAIRS // 2)
            transpose_group(last_b, SLOTS - 1, 0).then_inc(transposed, 1)
            gram_pair(last_b, PAIRS - 2, tiled=True)
            pe.wait_ge(e_act, BLOCKS * PAIRS // 2)
            tiled_gram(SLOTS - 2, 1)
            pe.wait_ge(e_last, 1)
            tiled_gram(SLOTS - 1, 1).then_inc(grams, 1)
            pe.wait_ge(h1_kept, LAST_PIECES + 3)
            layer2_early(0, range(N1))
            quarter_piece(QUARTERS - 1)
            layer2_early(1, range(N1 // 2))
            turn(LAST_PIECES + 3, units=P)
            layer2_early(1, range(N1 // 2, N1))
            pe.wait_ge(h1_kept, LAST_PIECES + 4)
            layer2_last()
            pe.wait_ge(h2_early_dve, 1)
            pe.wait_ge(h2_early_act, 1)
            for i in range(N2):
                last = nc.tensor.matmul(y_early, w3_sb[:, i:i + 1], h2[:, i, 0:EARLY],
                                        start=(i == 0), stop=(i == N2 - 1))
            last.then_inc(mm3_early, 1)
            pe.wait_ge(y_part_ready, 1)
            nc.tensor.matmul(y_last, y_part[:], tile_sum, start=True, stop=True).then_inc(mm3, 1)

        def move(copy, quarter, sample_quads, groups=range(GPQ)):
            for sq in sample_quads:
                for jq in range(JQ):
                    lo = 1 if jq == 0 else 0
                    col = FIELDS * sq + JJ * jq
                    src = g_ps[FIELDS * sq:FIELDS * (sq + 1), quarter % 2, groups[0]:groups[-1] + 1, col + lo:col + JJ]
                    at = quarter * QS + sq * GPQ
                    dst = z[FIELDS * jq:FIELDS * (jq + 1), lo:JJ, at + groups[0]:at + groups[-1] + 1]
                    last = copy(dst.rearrange("p j g -> p g j"), src)
            return last

        @block.vector
        def _(dve):
            dve.wait_ge(ids_loaded, 16)
            for dst, n, done in ((idx_now, SLOTS, idx_first), (row_idx, GROUPS, idx_all)):
                nc.vector.tensor_tensor(dst[:], ids_sb[:, 0:n], ids_sb[:, GROUPS:].to_broadcast([P, n]),
                                        ALU.add).then_inc(done, 1)

            def copy_pair(b, k):
                dve.wait_ge(transposed, b * PAIRS + k + 1)
                nc.vector.tensor_copy(e_t[:, k % 2], t_ps[:, k % 2]).then_inc(e_dve, 1)

            def move_quarter(b, q):
                dve.wait_ge(grams, b * QUARTERS + q + 1)
                move(nc.vector.tensor_copy, q, range(SPG // 2)).then_inc(z_dve, 1)

            def relu_h1(p, units=HID1 // 2):
                dve.wait_ge(mm1, p + 1)
                nc.vector.tensor_scalar(h1_s[:, 0:units], h1_acc[:, 0:units], 0.0, None, ALU.max).then_inc(relu1, 1)

            def relu2(b):
                dve.wait_ge(mm2, b + 1)
                nc.vector.tensor_scalar(h2[:, 0], h2_acc[0], b2_sb[:, 0:1], 0.0,
                                        ALU.add, ALU.max).then_inc(h2_dve, 1)

            def keep_y(b):
                dve.wait_ge(mm3, b + 1)
                nc.vector.tensor_copy(y_sb[:, bass.ds(b * BLOCK, BLOCK)], y_acc).then_inc(y_ready, 1)

            def run(b, first=False, is_last=False):
                for k in range(0, PAIRS, 2):
                    copy_pair(b, k)
                    if k % PPQ == 0:
                        if k > 0:
                            move_quarter(b, k // PPQ - 1)
                        elif not first:
                            move_quarter(b - 1, QUARTERS - 1)
                    if not first:
                        if NEXT_L1 // 2 == k // 2:
                            relu_h1(2 * b - 1)
                        elif L2 // 2 == k // 2:
                            relu2(b - 1)
                        elif L3 // 2 == k // 2:
                            keep_y(b - 1)
                    if not is_last and OWN_L1 // 2 == k // 2:
                        relu_h1(2 * b)
                    for q in range(QUARTERS - 1):
                        if is_last and LAST_L1[q] // 2 == k // 2:
                            relu_h1(LAST_PIECES + q, P)

            run(0, first=True)
            dve.wait_ge(top_loaded, 16 * 4)
            with dve.Fori(1, BLOCKS - 1) as b:
                run(b)
            run(BLOCKS - 1, is_last=True)
            dve.wait_ge(transposed, BLOCKS * PAIRS + 1)
            nc.vector.tensor_copy(e_t[:, 1, 1], t_ps[:, 0, 1]).then_inc(e_last, 1)
            dve.wait_ge(grams_half, 1)
            move(nc.vector.tensor_copy, QUARTERS - 1, range(SPG // 2), range(GPQ // 2))
            dve.wait_ge(grams, BLOCKS * QUARTERS)
            move(nc.vector.tensor_copy, QUARTERS - 1, range(SPG // 2), range(GPQ // 2, GPQ)).then_inc(z_dve, 1)
            dve.wait_ge(mm2_early, 1)
            nc.vector.tensor_scalar(h2[:, 0, 0:EARLY], h2_early[0], b2_sb[:, 0:1], 0.0,
                                    ALU.add, ALU.max).then_inc(h2_early_dve, 1)
            relu_h1(LAST_PIECES + 3, P)
            dve.wait_ge(mm2_last, 1)
            nc.vector.scalar_tensor_tensor(out=h2_w3[:], in0=h2_last, scalar=0.0, in1=w3_tile, op0=ALU.max,
                                           op1=ALU.mult, accum_out=y_part[:]).then_inc(y_part_ready, 1)
            dve.wait_ge(mm3, BLOCKS)
            nc.vector.tensor_copy(y_sb[:, BATCH - QS:], y_last).then_inc(y_ready, 1)

        @block.scalar
        def _(act):
            def copy_pair(b, k):
                act.wait_ge(transposed, b * PAIRS + k + 1)
                nc.scalar.copy(e_t[:, k % 2], t_ps[:, k % 2]).then_inc(e_act, 1)

            def move_quarter(b, q):
                act.wait_ge(grams, b * QUARTERS + q + 1)
                nc.scalar.copy(z[0:FIELDS, 0, q * QS:(q + 1) * QS],
                               dense_sb[:, bass.ds(b * BLOCK + q * QS, QS)])
                move(nc.scalar.copy, q, range(SPG // 2, SPG)).then_inc(z_act, 1)

            def relu2(b):
                act.wait_ge(mm2, b + 1)
                nc.scalar.activation(h2[:, 1], h2_acc[1], ACT.Relu, bias=b2_sb[:, 1:2]).then_inc(h2_act, 1)

            def keep_h1(p, at, samples, tiles):
                act.wait_ge(turned, p + 1)
                turns = N1 // tiles
                src = turned_acc[:, 0:turns * P].rearrange("p (u t s) -> p t u s", u=turns, t=tiles)
                dst = h1[:, :, at:at + samples].rearrange("p (t u) s -> p t u s", u=turns)
                for u in range(turns):
                    last = nc.scalar.copy(dst[:, :, u], src[:, :, u])
                last.then_inc(h1_kept, 1)

            def keep_piece(b, half):
                keep_h1(2 * b + half, half * 2 * QS, 2 * QS, 2)

            def refresh(b, q):
                nc.scalar.copy(idx_now[:, q * GPQ:(q + 1) * GPQ],
                               row_idx[:, bass.ds((b + 1) * SLOTS + q * GPQ, GPQ)]).then_inc(slots_free[q], 1)

            def run(b, first=False, is_last=False):
                for k in range(1, PAIRS, 2):
                    if is_last and k == PAIRS - 1:
                        keep_h1(LAST_PIECES + 2, (QUARTERS - 2) * QS, QS, SPG)
                        act.wait_ge(transposed, BLOCKS * PAIRS)
                        nc.scalar.copy(e_t[:, 1, 0], t_ps[:, 1, 0]).then_inc(e_act, 1)
                        act.wait_ge(grams_half, 1)
                        nc.scalar.copy(z[0:FIELDS, 0, EARLY:], dense_sb[:, BATCH - QS:])
                        move(nc.scalar.copy, QUARTERS - 1, range(SPG // 2, SPG), range(GPQ // 2))
                        continue
                    if k % PPQ == 1:
                        if k > PPQ:
                            move_quarter(b, k // PPQ - 1)
                        elif not first:
                            move_quarter(b - 1, QUARTERS - 1)
                    if k == L2 + 1 and not first:
                        relu2(b - 1)
                    copy_pair(b, k)
                    if k % PPQ == PPQ - 1 and not is_last:
                        refresh(b, k // PPQ)
                    if k == NEXT_TURN and not first:
                        keep_piece(b - 1, 1)
                    elif k == OWN_TURN and not is_last:
                        keep_piece(b, 0)
                    for q in range(QUARTERS - 2):
                        if is_last and LAST_TURN[q] // 2 == k // 2:
                            keep_h1(LAST_PIECES + q, q * QS, QS, SPG)

            act.wait_ge(dense_loaded, 16)
            act.wait_ge(idx_all, 1)
            run(0, first=True)
            act.wait_ge(top_loaded, 16 * 4)
            with act.Fori(1, BLOCKS - 1) as b:
                run(b)
            run(BLOCKS - 1, is_last=True)
            act.wait_ge(grams, BLOCKS * QUARTERS)
            move(nc.scalar.copy, QUARTERS - 1, range(SPG // 2, SPG), range(GPQ // 2, GPQ)).then_inc(z_act, 1)
            keep_h1(LAST_PIECES + 3, EARLY, QS, SPG)
            act.wait_ge(mm2_early, 2)
            nc.scalar.activation(h2[:, 1, 0:EARLY], h2_early[1], ACT.Relu, bias=b2_sb[:, 1:2]
                                 ).then_inc(h2_early_act, 1)
            act.wait_ge(mm3_early, 1)
            nc.scalar.copy(y_sb[:, BATCH - BLOCK:BATCH - QS], y_early).then_inc(y_early_ready, 1)


def kernel(**inputs):
    import numpy as np
    import concourse.bacc as bacc
    from concourse.bass_utils import run_bass_kernel_spmd

    tables = [np.asarray(inputs[f"tbl_{f}"]) for f in range(FIELDS)]
    starts = np.concatenate([[0], np.cumsum([t.shape[0] for t in tables])[:-1]]).astype(np.int32)
    ids = np.asarray(inputs["ids"]).reshape(BATCH // QS, SPG, GPQ, FIELDS).transpose(1, 3, 0, 2)
    ids = np.concatenate([ids.reshape(P, GROUPS), np.tile(starts, SPG).reshape(P, 1)], axis=1)
    w1 = np.asarray(inputs["W_top1"])
    pairs = FIELDS * (FIELDS - 1) // 2
    first, second = np.triu_indices(FIELDS, k=1)
    w1_z = np.zeros((JQ, FIELDS, JJ, HID1), w1.dtype)
    w1_z[second // JJ, first, second % JJ] = w1[:pairs]
    w1_z[0, :DENSE, 0] = w1[pairs:]
    w1_z[0, DENSE, 0] = np.asarray(inputs["b_top1"])
    dense = np.zeros((FIELDS, BATCH), np.asarray(inputs["dense_ctx"]).dtype)
    dense[:DENSE] = np.asarray(inputs["dense_ctx"]).T
    dense[DENSE] = 1.0
    b2, w3 = np.asarray(inputs["b_top2"]), np.asarray(inputs["W_top3"])
    tail = np.zeros((P, HID2 + 2 * QS + TU), w1.dtype)
    tail[0, :HID2] = b2
    tail[0, HID2:HID2 + QS] = 1.0
    tail[:, HID2 + QS:HID2 + 2 * QS] = np.tile(np.eye(QS), (SPG, 1))
    tail[:, HID2 + 2 * QS:] = np.repeat(w3.reshape(SPG, TU), QS, axis=0)
    arrays = {
        "ids": ids,
        "tables": np.concatenate(tables, axis=0),
        "dense": dense,
        "w1": w1_z.reshape(P, JJ, HID1),
        "w2": np.ascontiguousarray(np.asarray(inputs["W_top2"]).reshape(N1, P, HID2).transpose(1, 0, 2)),
        "b2": np.ascontiguousarray(b2.reshape(N2, P).T),
        "w3": np.ascontiguousarray(w3.reshape(N2, P).T),
        "tail": tail,
    }
    nc = bacc.Bacc("TRN2", target_bir_lowering=False, num_devices=1)
    args = [nc.dram_tensor(name, a.shape, mybir.dt.from_np(a.dtype), kind="ExternalInput").ap()
            for name, a in arrays.items()]
    out = nc.dram_tensor("y", (1, BATCH), F32, kind="ExternalOutput").ap()
    dlrm_tower(nc, *args, out)
    result = run_bass_kernel_spmd(nc, [arrays], core_ids=[0])
    return result.results[0]["y"].reshape(BATCH, 1)
```
